# Optimizing a Trainium2 kernel written in Bass

```python
import numpy as np
import jax
import jax.numpy as jnp

def _softmax(x, axis=-1):
    return jax.nn.softmax(x, axis=axis)

def _gelu(x):
    return jax.nn.gelu(x, approximate=True)

def _silu(x):
    return jax.nn.silu(x)

def _sigmoid(x):
    return jax.nn.sigmoid(x)

def _layernorm(x, axis=-1, eps=1e-05):
    m = jnp.mean(x, axis=axis, keepdims=True)
    v = jnp.var(x, axis=axis, keepdims=True)
    return (x - m) / jnp.sqrt(v + eps)

def _scatter_add(tgt, idx, src, axis=0):
    return tgt.at[idx].add(src)

def _segment_sum(src, seg, n):
    return jax.ops.segment_sum(src, seg, n)
kernel_name = 'mk_gnn_resnorm_d4_gnn_r8_e485f1'

def setup_inputs(seed: int=0):
    np.random.seed(seed)
    _w = jnp.asarray

    def _rec_inputs():
        import jax
        import jax.numpy as jnp
        _gk = jax.random.key(seed)
        x = -0.000202 + 1 * jax.random.normal(jax.random.fold_in(_gk, 1), (12500, 128), jnp.float32)
        _s = jax.random.randint(jax.random.fold_in(_gk, 2), (100000,), 0, 12500, jnp.int32)
        _d = jax.random.randint(jax.random.fold_in(_gk, 3), (100000,), 0, 12500, jnp.int32)
        _loop = jnp.arange(12500, dtype=jnp.int32)
        src = jnp.concatenate([_s, _d, _loop])
        dst = jnp.concatenate([_d, _s, _loop])
        _o = jnp.argsort(dst, stable=True)
        src = src[_o]
        dst = dst[_o]
        edge_attr_128 = 0.000167468 + 1.0002 * jax.random.normal(jax.random.fold_in(_gk, 12), (212500, 128), jnp.float32)
        edge_weight = jax.random.uniform(jax.random.fold_in(_gk, 15), (212500,), jnp.float32, 0.0, 0.799017)
        return (x, src, dst, edge_attr_128, edge_weight)
    x, src, dst, edge_attr_128, edge_weight = _rec_inputs()

    def _L0_gnn_setup():
        import jax, jax.numpy as jnp
        import numpy as np
        N_NODES = 6250
        N_EDGES = 100000
        DIM_IN = 128
        DIM_OUT = 128
        EPS = 1e-09

        def _branch(x, W, b, scale, offset, idx):
            h = jax.nn.relu(x @ W.T + b)
            mean = jnp.mean(h, axis=1, keepdims=True)
            var = jnp.var(h, axis=1, keepdims=True) + EPS
            d = h.shape[1]
            s = scale[idx * d:(idx + 1) * d]
            o = offset[idx * d:(idx + 1) * d]
            return (h - mean) * s * jax.lax.rsqrt(var) + o
        key = jax.random.key(seed)
        ks = jax.random.split(key, 8)
        feat_in = jax.random.normal(ks[0], (N_NODES, DIM_IN), dtype=jnp.float32)
        edge_row = jax.random.randint(ks[1], (N_EDGES,), 0, N_NODES, dtype=jnp.int32)
        edge_col = jax.random.randint(ks[2], (N_EDGES,), 0, N_NODES, dtype=jnp.int32)
        raw = jax.random.uniform(ks[3], (N_EDGES,), dtype=jnp.float32) + 0.1
        row_sum = jax.ops.segment_sum(raw, edge_row, num_segments=N_NODES)
        edge_val = raw / jnp.maximum(row_sum, EPS)[edge_row]
        W_self = jax.random.normal(ks[4], (DIM_OUT, DIM_IN), dtype=jnp.float32) * (1.0 / np.sqrt(DIM_IN))
        b_self = jax.random.normal(ks[5], (DIM_OUT,), dtype=jnp.float32) * 0.01
        W_neigh = jax.random.normal(ks[6], (DIM_OUT, DIM_IN), dtype=jnp.float32) * (1.0 / np.sqrt(DIM_IN))
        b_neigh = jax.random.normal(ks[7], (DIM_OUT,), dtype=jnp.float32) * 0.01
        scale = jnp.ones((2 * DIM_OUT,), dtype=jnp.float32)
        offset = jnp.zeros((2 * DIM_OUT,), dtype=jnp.float32)
        return {'feat_in': feat_in, 'edge_row': edge_row, 'edge_col': edge_col, 'edge_val': edge_val, 'W_self': W_self, 'b_self': b_self, 'W_neigh': W_neigh, 'b_neigh': b_neigh, 'scale': scale, 'offset': offset}
    _L0_gnn_all = _L0_gnn_setup()
    _L0_gnn_in = {k: v for k, v in _L0_gnn_all.items() if k in ('W_self', 'b_self', 'W_neigh', 'b_neigh', 'scale', 'offset')}
    del _L0_gnn_all

    def _L1_gnn_setup():
        import jax, jax.numpy as jnp
        import numpy as np
        N, E, D, H = (12500, 200000, 128, 32)
        BN_EPS = 1e-05
        NEG_SLOPE = 0.01

        def _bn(h, gamma, beta):
            m = h.mean(axis=0)
            v = h.var(axis=0)
            return (h - m) * jax.lax.rsqrt(v + BN_EPS) * gamma + beta

        def _gin_layer(x, src, dst, W1, b1, g1, be1, W2, b2, g2, be2):
            agg = jax.ops.segment_sum(x[src], dst, num_segments=x.shape[0])
            h = (x + agg) @ W1 + b1
            h = jnp.maximum(h, 0.0)
            h = _bn(h, g1, be1)
            h = h @ W2 + b2
            h = _bn(h, g2, be2)
            return jnp.where(h > 0, h, NEG_SLOPE * h)
        key = jax.random.key(seed)
        ks = jax.random.split(key, 8)
        x = jax.random.normal(ks[0], (N, D), jnp.float32)
        src = jax.random.randint(ks[1], (E,), 0, N, dtype=jnp.int32)
        dst = jax.random.randint(ks[2], (E,), 0, N, dtype=jnp.int32)

        def lin_w(k, fi, fo):
            s = 1.0 / np.sqrt(fi)
            return jax.random.uniform(k, (fi, fo), jnp.float32, -s, s)
        inp = {'x': x, 'src': src, 'dst': dst}
        wk = jax.random.split(ks[3], 4)
        for l in range(2):
            inp[f'W1_{l}'] = lin_w(wk[2 * l], D, H)
            inp[f'b1_{l}'] = jnp.zeros((H,), jnp.float32)
            inp[f'g1_{l}'] = jnp.ones((H,), jnp.float32)
            inp[f'be1_{l}'] = jnp.zeros((H,), jnp.float32)
            inp[f'W2_{l}'] = lin_w(wk[2 * l + 1], H, D)
            inp[f'b2_{l}'] = jnp.zeros((D,), jnp.float32)
            inp[f'g2_{l}'] = jnp.ones((D,), jnp.float32)
            inp[f'be2_{l}'] = jnp.zeros((D,), jnp.float32)
        return inp
    _L1_gnn_all = _L1_gnn_setup()
    _L1_gnn_in = {k: v for k, v in _L1_gnn_all.items() if k in ('W1_0', 'b1_0', 'g1_0', 'be1_0', 'W2_0', 'b2_0', 'g2_0', 'be2_0', 'W1_1', 'b1_1', 'g1_1', 'be1_1', 'W2_1', 'b2_1', 'g2_1', 'be2_1')}
    del _L1_gnn_all

    def _L2_gnn_setup():
        import jax, jax.numpy as jnp
        import numpy as np
        N_NODES = 2500
        N_EDGES = 40000
        D = 128
        LN_EPS = 1e-05
        key = jax.random.key(seed)
        k1, k2, k3, k4 = jax.random.split(key, 4)
        x = jax.random.normal(k1, (N_NODES, D), dtype=jnp.float32)
        edge_index = jax.random.randint(k2, (2, N_EDGES), 0, N_NODES, dtype=jnp.int64)
        edge_attr = jax.random.normal(k3, (N_EDGES, D), dtype=jnp.float32)
        W = jax.random.normal(k4, (3 * D, D), dtype=jnp.float32) / np.sqrt(3 * D)
        b = jnp.zeros((D,), dtype=jnp.float32)
        gamma = jnp.ones((D,), dtype=jnp.float32)
        beta = jnp.zeros((D,), dtype=jnp.float32)
        return {'x': x, 'edge_index': edge_index, 'edge_attr': edge_attr, 'W': W, 'b': b, 'gamma': gamma, 'beta': beta}
    _L2_gnn_all = _L2_gnn_setup()
    _L2_gnn_in = {k: v for k, v in _L2_gnn_all.items() if k in ('W', 'b', 'gamma', 'beta')}
    del _L2_gnn_all

    def _L3_gnn_setup():
        import jax, jax.numpy as jnp
        import numpy as np
        N_NODES = 6250
        N_EDGES = 100000
        IN_FEAT = 128
        UNITS = 128
        EPS = 1e-07
        LEAKY_SLOPE = 0.2
        key = jax.random.key(seed)
        k1, k2, k3, k4 = jax.random.split(key, 4)
        node_states = jax.random.normal(k1, (N_NODES, IN_FEAT), dtype=jnp.float32)
        edges = jax.random.randint(k2, (N_EDGES, 2), 0, N_NODES, dtype=jnp.int64)
        kernel = jax.random.normal(k3, (IN_FEAT, UNITS), dtype=jnp.float32) * 0.05
        kernel_attention = jax.random.normal(k4, (2 * UNITS, 1), dtype=jnp.float32) * 0.05
        return {'node_states': node_states, 'edges': edges, 'kernel': kernel, 'kernel_attention': kernel_attention}
    _L3_gnn_all = _L3_gnn_setup()
    _L3_gnn_in = {k: v for k, v in _L3_gnn_all.items() if k in ('kernel', 'kernel_attention')}
    del _L3_gnn_all
    return {'x': x, 'src': src, 'dst': dst, 'edge_attr_128': edge_attr_128, 'edge_weight': edge_weight, 'L0_gnn_W_self': _L0_gnn_in['W_self'], 'L0_gnn_b_self': _L0_gnn_in['b_self'], 'L0_gnn_W_neigh': _L0_gnn_in['W_neigh'], 'L0_gnn_b_neigh': _L0_gnn_in['b_neigh'], 'L0_gnn_scale': _L0_gnn_in['scale'], 'L0_gnn_offset': _L0_gnn_in['offset'], 'L1_gnn_W1_0': _L1_gnn_in['W1_0'], 'L1_gnn_b1_0': _L1_gnn_in['b1_0'], 'L1_gnn_g1_0': _L1_gnn_in['g1_0'], 'L1_gnn_be1_0': _L1_gnn_in['be1_0'], 'L1_gnn_W2_0': _L1_gnn_in['W2_0'], 'L1_gnn_b2_0': _L1_gnn_in['b2_0'], 'L1_gnn_g2_0': _L1_gnn_in['g2_0'], 'L1_gnn_be2_0': _L1_gnn_in['be2_0'], 'L1_gnn_W1_1': _L1_gnn_in['W1_1'], 'L1_gnn_b1_1': _L1_gnn_in['b1_1'], 'L1_gnn_g1_1': _L1_gnn_in['g1_1'], 'L1_gnn_be1_1': _L1_gnn_in['be1_1'], 'L1_gnn_W2_1': _L1_gnn_in['W2_1'], 'L1_gnn_b2_1': _L1_gnn_in['b2_1'], 'L1_gnn_g2_1': _L1_gnn_in['g2_1'], 'L1_gnn_be2_1': _L1_gnn_in['be2_1'], 'L2_gnn_W': _L2_gnn_in['W'], 'L2_gnn_b': _L2_gnn_in['b'], 'L2_gnn_gamma': _L2_gnn_in['gamma'], 'L2_gnn_beta': _L2_gnn_in['beta'], 'L3_gnn_kernel': _L3_gnn_in['kernel'], 'L3_gnn_kernel_attention': _L3_gnn_in['kernel_attention']}

def reference(x, src, dst, edge_attr_128, edge_weight, L0_gnn_W_self, L0_gnn_b_self, L0_gnn_W_neigh, L0_gnn_b_neigh, L0_gnn_scale, L0_gnn_offset, L1_gnn_W1_0, L1_gnn_b1_0, L1_gnn_g1_0, L1_gnn_be1_0, L1_gnn_W2_0, L1_gnn_b2_0, L1_gnn_g2_0, L1_gnn_be2_0, L1_gnn_W1_1, L1_gnn_b1_1, L1_gnn_g1_1, L1_gnn_be1_1, L1_gnn_W2_1, L1_gnn_b2_1, L1_gnn_g2_1, L1_gnn_be2_1, L2_gnn_W, L2_gnn_b, L2_gnn_gamma, L2_gnn_beta, L3_gnn_kernel, L3_gnn_kernel_attention):
    import jax
    import jax.numpy as jnp

    def _L0_gnn_ref(feat_in, edge_row, edge_col, edge_val, W_self, b_self, W_neigh, b_neigh, scale, offset):
        import jax, jax.numpy as jnp
        import numpy as np
        N_NODES = 6250
        N_EDGES = 100000
        DIM_IN = 128
        DIM_OUT = 128
        EPS = 1e-09

        def _branch(x, W, b, scale, offset, idx):
            h = jax.nn.relu(x @ W.T + b)
            mean = jnp.mean(h, axis=1, keepdims=True)
            var = jnp.var(h, axis=1, keepdims=True) + EPS
            d = h.shape[1]
            s = scale[idx * d:(idx + 1) * d]
            o = offset[idx * d:(idx + 1) * d]
            return (h - mean) * s * jax.lax.rsqrt(var) + o
        n = feat_in.shape[0]
        feat_neigh = jax.ops.segment_sum(edge_val[:, None] * feat_in[edge_col], edge_row, num_segments=n)
        feat_self_trans = _branch(feat_in, W_self, b_self, scale, offset, 0)
        feat_neigh_trans = _branch(feat_neigh, W_neigh, b_neigh, scale, offset, 1)
        return feat_self_trans + feat_neigh_trans

    def _L1_gnn_ref(x, src, dst, W1_0, b1_0, g1_0, be1_0, W2_0, b2_0, g2_0, be2_0, W1_1, b1_1, g1_1, be1_1, W2_1, b2_1, g2_1, be2_1):
        import jax, jax.numpy as jnp
        import numpy as np
        N, E, D, H = (12500, 200000, 128, 32)
        BN_EPS = 1e-05
        NEG_SLOPE = 0.01

        def _bn(h, gamma, beta):
            m = h.mean(axis=0)
            v = h.var(axis=0)
            return (h - m) * jax.lax.rsqrt(v + BN_EPS) * gamma + beta

        def _gin_layer(x, src, dst, W1, b1, g1, be1, W2, b2, g2, be2):
            agg = jax.ops.segment_sum(x[src], dst, num_segments=x.shape[0])
            h = (x + agg) @ W1 + b1
            h = jnp.maximum(h, 0.0)
            h = _bn(h, g1, be1)
            h = h @ W2 + b2
            h = _bn(h, g2, be2)
            return jnp.where(h > 0, h, NEG_SLOPE * h)
        h = _gin_layer(x, src, dst, W1_0, b1_0, g1_0, be1_0, W2_0, b2_0, g2_0, be2_0)
        h = _gin_layer(h, src, dst, W1_1, b1_1, g1_1, be1_1, W2_1, b2_1, g2_1, be2_1)
        return h

    def _L2_gnn_ref(x, edge_index, edge_attr, W, b, gamma, beta):
        import jax, jax.numpy as jnp
        import numpy as np
        N_NODES = 2500
        N_EDGES = 40000
        D = 128
        LN_EPS = 1e-05
        row, col = (edge_index[0], edge_index[1])
        msg_in = jnp.concatenate([x[row], x[col], edge_attr], axis=-1)
        h = msg_in @ W + b
        mu = jnp.mean(h, axis=-1, keepdims=True)
        var = jnp.mean(jnp.square(h - mu), axis=-1, keepdims=True)
        h = (h - mu) * jax.lax.rsqrt(var + LN_EPS) * gamma + beta
        msg = jax.nn.relu(h)
        out = jax.ops.segment_sum(msg, row, num_segments=x.shape[0])
        return out

    def _L3_gnn_ref(node_states, edges, kernel, kernel_attention):
        import jax, jax.numpy as jnp
        import numpy as np
        N_NODES = 6250
        N_EDGES = 100000
        IN_FEAT = 128
        UNITS = 128
        EPS = 1e-07
        LEAKY_SLOPE = 0.2
        n_nodes = node_states.shape[0]
        units = kernel.shape[1]
        h = node_states @ kernel
        edge_states = h[edges].reshape(edges.shape[0], 2 * units)
        scores = jax.nn.leaky_relu(edge_states @ kernel_attention, negative_slope=LEAKY_SLOPE)[:, 0]
        scores_exp = jnp.exp(jnp.clip(scores, -2.0, 2.0))
        tgt = edges[:, 0]
        denom = jax.ops.segment_sum(scores_exp, tgt, num_segments=n_nodes)
        alpha = scores_exp / (denom[tgt] + EPS)
        neigh = h[edges[:, 1]]
        out = jax.ops.segment_sum(neigh * alpha[:, None], tgt, num_segments=n_nodes)
        return out
    edge_index = jnp.stack([src, dst])
    edge_index_t = jnp.stack([src, dst], axis=1)
    x = _layernorm(x + _L0_gnn_ref(x, src, dst, edge_weight, L0_gnn_W_self, L0_gnn_b_self, L0_gnn_W_neigh, L0_gnn_b_neigh, L0_gnn_scale, L0_gnn_offset), axis=-1)
    x = _layernorm(x + _L1_gnn_ref(x, src, dst, L1_gnn_W1_0, L1_gnn_b1_0, L1_gnn_g1_0, L1_gnn_be1_0, L1_gnn_W2_0, L1_gnn_b2_0, L1_gnn_g2_0, L1_gnn_be2_0, L1_gnn_W1_1, L1_gnn_b1_1, L1_gnn_g1_1, L1_gnn_be1_1, L1_gnn_W2_1, L1_gnn_b2_1, L1_gnn_g2_1, L1_gnn_be2_1), axis=-1)
    x = _layernorm(x + _L2_gnn_ref(x, edge_index, edge_attr_128, L2_gnn_W, L2_gnn_b, L2_gnn_gamma, L2_gnn_beta), axis=-1)
    x = _layernorm(x + _L3_gnn_ref(x, edge_index_t, L3_gnn_kernel, L3_gnn_kernel_attention), axis=-1)
    return x

_drawn_inputs = setup_inputs


def setup_inputs(seed=0):
    import zlib

    import numpy as np

    out = dict(_drawn_inputs(seed))
    spreads = {'L0_gnn_scale': (1.0, 0.2),
     'L0_gnn_offset': (0.0, 0.1),
     'L1_gnn_b1_0': (0.0, 0.47),
     'L1_gnn_g1_0': (1.0, 0.2),
     'L1_gnn_be1_0': (0.0, 0.8),
     'L1_gnn_b2_0': (0.0, 0.8),
     'L1_gnn_g2_0': (1.0, 0.2),
     'L1_gnn_be2_0': (0.0, 0.1),
     'L1_gnn_b1_1': (0.0, 0.315),
     'L1_gnn_g1_1': (1.0, 0.2),
     'L1_gnn_be1_1': (0.0, 0.8),
     'L1_gnn_b2_1': (0.0, 0.8),
     'L1_gnn_g2_1': (1.0, 0.2),
     'L1_gnn_be2_1': (0.0, 0.1),
     'L2_gnn_b': (0.0, 0.1),
     'L2_gnn_gamma': (1.0, 0.2),
     'L2_gnn_beta': (0.0, 0.1)}
    factors = {'L0_gnn_b_self': 3.366, 'L0_gnn_b_neigh': 7.294}
    for name, (base, spread) in spreads.items():
        noise = np.random.default_rng([zlib.crc32(name.encode()), seed]).standard_normal(out[name].shape)
        drawn = base * np.exp(spread * noise) if base else spread * noise
        out[name] = jnp.asarray(drawn.astype(out[name].dtype))
    for name, factor in factors.items():
        out[name] = (out[name] * factor).astype(out[name].dtype)
    return out
```

```python
from contextlib import ExitStack

import numpy as np

import concourse.bass as bass
from concourse import mybir

ALU = mybir.AluOpType
ACT = mybir.ActivationFunctionType
F32 = mybir.dt.float32
BF16 = mybir.dt.bfloat16
I32 = mybir.dt.int32
U16 = mybir.dt.uint16
ONLY_DVE = (mybir.EngineType.DVE,)
ONLY_PE = (mybir.EngineType.PE,)
P = 128
BANK = 512


class OrderSems:

    def __init__(self, nth, both, sem):
        self.nth = nth
        self.eqh = both["eqh"]
        self.hist = both["hist"]
        self.eqp = both["eqp"]
        self.pos = both["pos"]
        self.took = both["took"]
        self.nt = both["nt"]
        self.start = both["start"]
        self.cmp = both["cmp"]
        self.blkmm = both["blkmm"]
        self.ranked = both["ranked"]
        self.staged = both["staged"]
        self.attr0 = both["attr0"]
        self.attr1 = both["attr1"]
        self.scatt = both["scatt"]
        self.scat0 = sem(f"scat0_{nth}")
        self.scat1 = sem(f"scat1_{nth}")


class PassSems:

    def __init__(self, nth, first, own, got, got0):
        self.nth, self.first, self.got0 = nth, first, got0
        self.got = got
        self.zero = own["zero"]
        self.idx = own["idx"]
        self.oh = own["oh"]
        self.mm = own["mm"]
        self.acc = own["acc"]


class MlpSems(PassSems):

    def __init__(self, own, got, got0, lo, lo0, attr):
        PassSems.__init__(self, 0, 0, own, got, got0)
        self.lo, self.lo0 = lo, lo0
        self.attr = attr
        self.oht = own["oht"]
        self.tr = own["tr"]
        self.trc = own["trc"]
        self.hmm = own["hmm"]
        self.var = own["var"]
        self.std = own["std"]
        self.hch = own["hch"]
        self.hid = own["hid"]
        self.msg = own["msg"]


class AttentionSems(PassSems):

    def __init__(self, own, got, got0, lo, lo0):
        PassSems.__init__(self, 0, 0, own, got, got0)
        self.lo, self.lo0 = lo, lo0
        self.oht = own["oht"]
        self.smm = own["smm"]
        self.sc = own["sc"]
        self.exp = own["exp"]


class NodeSems:

    def __init__(self, n, sem):
        self.var = sem(f"n{n}_var")
        self.std = sem(f"n{n}_std")
        self.ch = sem(f"n{n}_ch")
        self.xnew = sem(f"n{n}_xnew")
        self.xl = [sem(f"n{n}_xl{k}") for k in range(2)]
        self.st = [sem(f"n{n}_st{k}") for k in range(2)]
        if n != 4:
            self.ptr = sem(f"n{n}_ptr")
            self.ptrc = sem(f"n{n}_ptrc")
            self.pmm = sem(f"n{n}_pmm")
            self.pev = sem(f"n{n}_pev")
            self.tab = [sem(f"n{n}_tab{k}") for k in range(2)]
        if n in (0, 2):
            self.tr = sem(f"n{n}_tr")
        if n == 0:
            self.trc = sem("n0_trc")
            self.hmm = sem("n0_hmm")
            self.relu = sem("n0_relu")
        if n == 3:
            self.one = sem("n3_one")


class GinSems:

    def __init__(self, sem):
        self.u = sem("gin_u")
        self.tr = sem("gin_tr")
        self.relu = sem("gin_relu")
        self.ch = sem("gin_ch")
        self.var = sem("gin_var")
        self.std = sem("gin_std")
        self.aff = sem("gin_aff")
        self.hbn = sem("gin_hbn")
        self.mm = sem("gin_mm")
        self.ev = sem("gin_ev")
        self.ybn = sem("gin_ybn")
        self.act = sem("gin_act")
        self.zmm = sem("gin_zmm")
        self.zev = sem("gin_zev")
        self.tab = sem("gin_tab")


def wait(eng, sem, value):
    if not isinstance(value, int) or value > 0:
        eng.wait_ge(sem, value)


class Chain:

    def __init__(self, eng, sem):
        self.eng, self.sem, self.base, self.n = eng, sem, 0, 0

    def begin(self, base):
        self.base, self.n = base, 0

    def post(self, ins):
        self.n += 1
        ins.then_inc(self.sem, 1)

    def sync(self):
        wait(self.eng, self.sem, self.base + self.n)

    def __call__(self, ins):
        self.post(ins)
        self.sync()


def gnn_program(nc, t, out):
    x, src, dst = t["x"], t["src"], t["dst"]
    edge_attr, edge_weight = t["edge_attr_128"], t["edge_weight"]
    N, D = x.shape
    E = src.shape[0]
    H = t["L1_gnn_W1_0"].shape[1]
    NB = -(-N // P)
    NP = NB * P
    EC = E // P
    ETAIL = E - EC * P
    COLS = EC + 1
    SG = 10
    SGROUPS = EC // SG
    assert SGROUPS * SG == EC and SGROUPS % 2 == 0 and ETAIL > 0
    G = 4
    RING = 8
    BODY = G * RING
    TILES = -(-((E + NB * (P - 1)) // P) // BODY) * BODY
    GROUPS = TILES // G
    ITERS = TILES // BODY
    FA, FB = 3, 2
    EROW = D + FA
    HROW = D + 2
    ACCW = 132
    BSTEP = 7
    NSTEPS = NB // BSTEP
    assert NSTEPS * BSTEP == NB and NSTEPS % 2 == 0
    NCH = 25
    CH = N // NCH
    assert CH * NCH == N and CH <= BANK
    CHUNKS = [(c, min(BANK, COLS - c)) for c in range(0, COLS, BANK)]
    NOKEY = 1 << 20

    ctx = ExitStack()
    with ctx:
        def sb(name, shape, dt=F32):
            return ctx.enter_context(nc.sbuf_tensor(name, shape, dt))

        def sem(name):
            return ctx.enter_context(nc.semaphore(name))

        def dram(name, shape, dt=F32):
            return nc.dram_tensor(name, shape, dt, kind="Internal").ap()

        x_pad = dram("x_pad", (NP, D))
        x1_tab = dram("x1_tab", (NP, D))
        x2_tab = dram("x2_tab", (NP, D))
        x3_tab = dram("x3_tab", (NP, D))
        z_tab = [dram("z0_tab", (NP, H)), dram("z1_tab", (NP, H))]
        q_tab = dram("q_tab", (NP, D))
        h_tab = dram("h_tab", (NP, HROW))
        edges_a = dram("edges_a", (P * TILES, EROW))
        edges_b = dram("edges_b", (P * TILES, FB))
        lo_rows = dram("lo_rows", (TILES * P,))
        blk_b_dram = dram("blk_b_dram", (1, TILES), I32)

        pool_words = 2 * 12936
        big = sb("big", [P, pool_words])
        work = sb("work", [P, 14720])
        pay_a = sb("pay_a", [P, TILES, FA])
        blk_a = sb("blk_a", [1, TILES], I32)

        def carver(region, start):
            at = [start]

            def take(shape, dt=F32):
                n = int(np.prod(shape))
                words = n if dt in (F32, I32) else n // 2
                v = region[:, at[0]:at[0] + words]
                at[0] += words
                assert at[0] <= region.shape[1], (at[0], region.shape)
                if dt is not F32:
                    v = v.bitcast(dt)
                if len(shape) == 2:
                    v = v.rearrange("p (a b) -> p a b", a=shape[0])
                elif len(shape) == 3:
                    v = v.rearrange("p (a b c) -> p a b c", a=shape[0], b=shape[1])
                return v
            return take

        acc = big[:, 0:NB * ACCW]
        side = big[:, NB * ACCW:2 * NB * ACCW]
        p_all = side[:, 0:NP]
        z_all = side[:, 0:NB * H]
        h_all = side[0:H, 0:NP]
        y_all = acc[:, 0:NP]

        ident = sb("ident", [P, P])
        iota = sb("iota", [P, P])
        iota_p = sb("iota_p", [P, 1])
        ones = sb("ones", [P, P])
        before_f = sb("before_f", [P, P])
        before_h = sb("before_h", [P, P], BF16)
        onecol = sb("onecol", [P, 2 * P], BF16)
        ws_t = sb("ws_t", [P, D])
        wn_t = sb("wn_t", [P, D])
        bias0 = sb("bias0", [1, 2 * D])
        scale0 = sb("scale0", [P, 2 * D])
        offs0 = sb("offs0", [P, D])
        w1 = [sb(f"w1_{n}", [P, H]) for n in range(2)]
        w2 = [sb(f"w2_{n}", [H, D]) for n in range(2)]
        col_h = [sb(f"col_h{n}", [H, 3]) for n in range(2)]
        col_d = [sb(f"col_d{n}", [P, 3]) for n in range(2)]
        wc = sb("wc", [P, 3, D])
        b2c = sb("b2c", [1, D])
        gamma2 = sb("gamma2", [P, D])
        beta2 = sb("beta2", [P, D])
        kaug = sb("kaug", [P, HROW])
        ka = sb("ka", [P, 2])
        a_all = sb("a_all", [P, NB])
        small = sb("small", [P, 16])
        small_i = sb("small_i", [P, 4], I32)
        eps2 = sb("eps2", [P, 1])
        spread = sb("spread", [P, 4, 3, G])
        square = sb("square", [P, G, P])

        ps = ctx.enter_context(nc.psum_tensor("ps", [P, 8, BANK], F32))

        take = carver(big, 0)
        key_i = [take((COLS,), I32), take((COLS,), I32)]
        wt = take((COLS,))
        hi_i = take((COLS,), I32)
        lo_i = [take((COLS,), I32), take((COLS,), I32)]
        pos_f = take((COLS,))
        pos_i = [take((COLS,), I32), take((COLS,), I32)]
        LOT0 = 9 * COLS
        scan = [take((COLS,)), take((COLS,))]
        base = take((COLS,))
        eq = take((2, COLS + 1), BF16)
        cmp_tiles = eq.rearrange("p a c -> p (a c)")[:, 0:TILES]
        tile_no = take((TILES,))
        block_row = take((2, P))
        raw = take((4, P))
        raw_offs = take((2 * D,))
        hi_h = take((COLS + 1,), BF16)[:, 0:COLS]
        take = carver(work, 0)
        stage_a = take((2, SG * EROW)).rearrange("p s (j f) -> p s j f", f=EROW)
        stage_b = take((2, SG * FB)).rearrange("p s (j f) -> p s j f", f=FB)
        stage_pos = take((2, SG), I32)
        FILL = 44
        fill_a = take((FILL, EROW))
        fill_b = take((TILES, FB))

        take = carver(work, 0)
        rows = take((RING * G * HROW,))
        idx = take((RING, G), I32)
        pst = take((RING, G, FA))
        onehot = take((4, G, P))
        lo_bc = take((4, G * P))
        onehot_t = take((2, G * P))
        score = take((2, 4, G))
        attr = take((4, G, D))
        attr_t = take((2, G * P))
        hid = take((2, G, D))
        msg = take((2, G, D))
        take = carver(work, 9400)
        pay_b = take((TILES, FB))
        blk_b = take((TILES,), I32)[0:1, :]

        take = carver(work, 0)
        xin = take((2, BSTEP, D))
        feat_t = take((2, BSTEP, 2 * D))
        hidn = take((2, BSTEP, 2 * D))
        xnew = take((2, BSTEP, D))
        tabrow = take((2, BSTEP * HROW))
        stats = take((2 * BSTEP, 6))
        mom = [take((2 * BSTEP,)) for _ in range(8)]
        proj_t = take((2, BSTEP * D))
        take = carver(work, 0)
        bn_part = take((NCH, 6))
        bn_cols = take((8,))

        s_ident, s_onecol, s_before, s_fillsrc, s_init = (sem(n) for n in
            ("s_ident", "s_onecol", "s_before", "s_fillsrc", "s_init"))
        s_keyin, s_win, s_xpad, s_fill = (sem(n) for n in
            ("s_keyin", "s_win", "s_xpad", "s_fill"))
        s_prep, s_prep_mm = sem("s_prep"), sem("s_prep_mm")
        pool_begun, pe_begun, dve_begun = sem("pool_begun"), sem("pe_begun"), sem("dve_begun")
        s_sort = sem("s_sort")
        both = {k: sem(f"sort_{k}") for k in ("eqh", "hist", "eqp", "pos", "took", "nt", "start", "cmp", "blkmm",
                                              "ranked", "staged", "attr0", "attr1", "scatt")}
        orders = [OrderSems(n, both, sem) for n in range(2)]
        s_pay_a, s_pay_b, s_lot, s_lotc, s_lost, s_blkst = (sem(n) for n in
            ("s_pay_a", "s_pay_b", "s_lot", "s_lotc", "s_lost", "s_blkst"))

        got = [sem(f"got{h}") for h in range(RING)]

        lo_in = [sem(f"lo_in{h}") for h in range(4)]
        attr_in_sems = [sem(f"attr_in{h}") for h in range(4)]
        simple = {k: sem(f"sum_{k}") for k in ("zero", "idx", "oh", "mm", "acc")}

        names = ("zero", "idx", "oh", "mm", "acc", "oht")
        per_pass = ITERS * G * 16
        p0, p1, p2 = (PassSems(n, n * GROUPS, simple, got, n * per_pass) for n in range(3))
        p3 = MlpSems({k: sem(f"p3_{k}") for k in names + ("tr", "trc", "hmm", "var", "std", "hch", "hid", "msg")},
                     got, 3 * per_pass, lo_in, 0, attr_in_sems)
        p4 = AttentionSems({k: sem(f"p4_{k}") for k in names + ("smm", "sc", "exp")},
                           got, 4 * per_pass, lo_in, GROUPS // 4 * 16)
        n0, n2, n3, n4 = (NodeSems(n, sem) for n in (0, 2, 3, 4))
        gin = GinSems(sem)

        edges_a_v = edges_a.rearrange("(p t) f -> p t f", p=P)
        edges_b_v = edges_b.rearrange("(p t) f -> p t f", p=P)
        attr_v = edge_attr[0:EC * P, :].rearrange("(p t) f -> p t f", p=P)

        def blocks_of(table, s):
            return table[bass.ds(s * (BSTEP * P), BSTEP * P), :].rearrange("(b p) f -> p b f", p=P)

        def run_steps(eng, steps, unroll, lag, step):
            for s in range(unroll):
                step(s, s, 0)
            with eng.Fori(1, steps // unroll) as i:
                for k in range(unroll):
                    step(i * unroll + k, k, i)
            for s in range(steps, steps + lag):
                step(s, s % unroll, s // unroll)

        def write_out(steps, unroll, lag, step):
            for s in range(steps + lag):
                step(s, s % unroll, s // unroll)

        def live(s, n):
            return not isinstance(s, int) or 0 <= s < n

        def back(k, u, lag, unroll):
            return (k - lag) % unroll, u + (k - lag) // unroll

        def load_blocks(eng_type, blk, g):
            _, v = nc.values_load_multi_w_load_instructions(
                blk[0:1, bass.ds(g * G, G)], eng_type, min_val=0, max_val=NB - 1,
                skip_runtime_bounds_check_because="each tile belongs to one of the NB blocks")
            return v

        def hidden_bank(k):
            return ps[:, (2, 3, 6, 7)[k % 4], :]

        def bank_slot(k):
            return ps[:, 4 * k:4 * k + 4, :].rearrange("p a b -> p (a b)")

        block = ctx.enter_context(nc.Block())

        weight_loads = [
            (raw[:, 0, :], t["L0_gnn_W_self"]), (raw[:, 1, :], t["L0_gnn_W_neigh"]),
            (raw[:, 2, :], t["L3_gnn_kernel"]), (kaug[:, 0:D], t["L3_gnn_kernel"]),
            (ka[:, 0:1], t["L3_gnn_kernel_attention"][0:P, :]), (ka[:, 1:2], t["L3_gnn_kernel_attention"][P:2 * P, :]),
            (bias0[:, 0:D], t["L0_gnn_b_self"].rearrange("(o f) -> o f", o=1)),
            (bias0[:, D:2 * D], t["L0_gnn_b_neigh"].rearrange("(o f) -> o f", o=1)),
            (scale0[:, :], t["L0_gnn_scale"].partition_broadcast(P)),
            (raw_offs, t["L0_gnn_offset"].partition_broadcast(P)),
            (wc[:, :, :], t["L2_gnn_W"].rearrange("(k p) f -> p k f", p=P)),
            (b2c[:, :], t["L2_gnn_b"].rearrange("(o f) -> o f", o=1)),
            (gamma2[:, :], t["L2_gnn_gamma"].partition_broadcast(P)),
            (beta2[:, :], t["L2_gnn_beta"].partition_broadcast(P)),
        ]
        for l in range(2):
            weight_loads += [(w1[l][:, :], t[f"L1_gnn_W1_{l}"]), (w2[l][:, :], t[f"L1_gnn_W2_{l}"])]
            for c, v in enumerate(("b1", "g1", "be1")):
                weight_loads.append((col_h[l][:, c:c + 1], t[f"L1_gnn_{v}_{l}"].rearrange("(f o) -> f o", o=1)))
            for c, v in enumerate(("b2", "g2", "be2")):
                weight_loads.append((col_d[l][:, c:c + 1], t[f"L1_gnn_{v}_{l}"].rearrange("(f o) -> f o", o=1)))
        PREP = 11
        WIN = 16 * len(weight_loads)
        lot_tmp = big[0:TILES // 16, LOT0:LOT0 + 16 * P].rearrange("t (c p) -> t c p", p=P)

        def node_sp(sp, n, table, to, kind):
            before = {0: None, 2: n0, 3: n2, 4: n3}[kind]
            if before is None:
                sp.wait_ge(s_xpad, 32)
            else:
                for k in range(2):
                    sp.wait_ge(before.st[k], NSTEPS // 2 * 16)
                    sp.wait_ge(before.tab[k], NSTEPS // 2 * 16)
            {0: lambda: sp.wait_ge(p0.acc, TILES), 2: lambda: sp.wait_ge(gin.act, 10),
             3: lambda: sp.wait_ge(p3.acc, TILES), 4: lambda: sp.wait_ge(p4.acc, TILES)}[kind]()

            def step(s, k, u):
                if live(s, NSTEPS):
                    wait(sp, n.xnew, s - 1)
                    if kind == 0:
                        wait(sp, n.tr, s - 1)
                    sp.dma_start(xin[:, k], blocks_of(table, s)).then_inc(n.xl[k], 16)
                g, (kk, _) = s - 2, back(k, u, 2, 2)
                if live(g, NSTEPS):
                    wait(sp, n.xnew, g + 1)
                    if kind == 4 and isinstance(g, int) and g == NSTEPS - 1:
                        full, part = N // P - g * BSTEP, N % P
                        row = g * BSTEP * P
                        sp.dma_start(to[row:row + full * P, :].rearrange("(b p) f -> p b f", p=P),
                                     xnew[:, kk, 0:full]).then_inc(n.st[kk], 16)
                        sp.dma_start(to[row + full * P:N, :], xnew[0:part, kk, full]).then_inc(n.st[kk], 16)
                    else:
                        sp.dma_start(blocks_of(to, g), xnew[:, kk]).then_inc(n.st[kk], 16)
                    if kind != 4:
                        wait(sp, n.pev, g + 1)
                        if kind == 0:
                            tab, row = z_tab[0], z_all[:, bass.ds(g * (BSTEP * H), BSTEP * H)].rearrange("p (b f) -> p b f", f=H)
                        elif kind == 2:
                            tab, row = q_tab, tabrow[:, kk, 0:BSTEP * D].rearrange("p (b f) -> p b f", f=D)
                        else:
                            tab, row = h_tab, tabrow[:, kk].rearrange("p (b f) -> p b f", f=HROW)
                        sp.dma_start(blocks_of(tab, g), row).then_inc(n.tab[kk], 16)
            run_steps(sp, NSTEPS, 2, 2, step)

        @block.sync
        def _(sp):
            sp.wait_ge(s_init, 1)
            for n, (view, arr) in enumerate(((key_i[0], src), (key_i[1], dst), (wt, edge_weight))):
                sp.dma_start(view[:, 0:EC], arr[0:EC * P].rearrange("(p t) -> p t", p=P)).then_inc(s_keyin, 16)
                sp.dma_start(view[0:ETAIL, EC:COLS],
                             arr[EC * P:E].rearrange("(p o) -> p o", o=1)).then_inc(s_keyin, 16)
            for dst_ap, src_ap in weight_loads:
                sp.dma_start(dst_ap, src_ap).then_inc(s_win, 16)
            sp.wait_ge(s_fillsrc, 4)
            with sp.Fori(0, TILES // FILL) as i:
                sp.dma_start(edges_a_v[:, bass.ds(i * FILL, FILL), :], fill_a).then_inc(s_fill, 16)
            sp.dma_start(edges_b_v, fill_b).then_inc(s_fill, 16)
            sp.dma_start(x_pad[N:NP, :], fill_a[0:NP - N, 0, 0:D]).then_inc(s_xpad, 16)
            sp.dma_start(x_pad[0:N, :], x).then_inc(s_xpad, 16)

            oa = orders[0]

            def attr_in(s, k, u):
                wait(sp, (oa.scat0, oa.scat1)[k], u * (16 * SG))
                sp.dma_start(stage_a[:, k, :, 0:D], attr_v[:, bass.ds(s * SG, SG), :]).then_inc((oa.attr0, oa.attr1)[k], 16)
            run_steps(sp, SGROUPS, 2, 0, attr_in)
            sp.wait_ge(oa.scat0, SGROUPS // 2 * 16 * SG)
            sp.dma_start(stage_a[0:ETAIL, 0, 0, 0:D], edge_attr[EC * P:E, :]).then_inc(oa.attr0, 16)

            sp.wait_ge(oa.scat1, SGROUPS // 2 * 16 * SG)
            sp.wait_ge(oa.scatt, 16)
            for c in range(4):
                part = slice(c * (TILES // 4), (c + 1) * (TILES // 4))
                sp.dma_start(pay_a[:, part, :], edges_a_v[:, part, D:EROW],
                             allow_slow_non_contiguous=True).then_inc(s_pay_a, 16)
            sp.wait_ge(orders[1].ranked, 2)
            sp.dma_start(blk_b_dram, tile_no.bitcast(I32)[0:1, :]).then_inc(s_blkst, 16)
            sp.wait_ge(s_lotc, 16)
            sp.dma_start(lo_rows.rearrange("(c t p) -> t c p", p=P, c=16), lot_tmp).then_inc(s_lost, 16)

            node_sp(sp, n0, x_pad, x1_tab, 0)
            sp.wait_ge(s_blkst, 16)
            sp.wait_ge(n0.tab[0], NSTEPS // 2 * 16)
            sp.wait_ge(n0.tab[1], NSTEPS // 2 * 16)
            sp.dma_start(pay_b, edges_b_v).then_inc(s_pay_b, 16)
            sp.dma_start(blk_b, blk_b_dram).then_inc(s_pay_b, 16)
            g0 = gin
            for s in range(NSTEPS):
                sp.wait_ge(g0.zev, s + 1)
                sp.dma_start(blocks_of(z_tab[1], s),
                             z_all[:, s * BSTEP * H:(s + 1) * BSTEP * H].rearrange("p (b f) -> p b f", f=H)).then_inc(g0.tab, 16)
            node_sp(sp, n2, x1_tab, x2_tab, 2)

            def edge_in(p, attrs):
                def step(s, k, u):
                    n = (u * 2 + k // 4) if isinstance(u, int) else u * 2 + k // 4
                    if attrs:
                        wait(sp, p.tr, s - 3)
                        sp.dma_start(attr[:, k % 4], edges_a_v[:, bass.ds(s * G, G), 0:D]).then_inc(p.attr[k % 4], 16)
                    wait(sp, p.oht, s - 3)
                    sp.dma_start(lo_bc[:, k % 4, :], lo_rows[bass.ds(s * (G * P), G * P)].partition_broadcast(P)).then_inc(p.lo[k % 4], 16)
                run_steps(sp, GROUPS, RING, 0, step)
            sp.wait_ge(n2.pev, NSTEPS)
            sp.wait_ge(s_lost, 16)
            edge_in(p3, True)
            node_sp(sp, n3, x2_tab, x3_tab, 3)
            sp.wait_ge(n3.pev, NSTEPS)
            for k in range(2):
                sp.wait_ge(n3.tab[k], NSTEPS // 2 * 16)
                sp.wait_ge(n3.st[k], NSTEPS // 2 * 16)
            edge_in(p4, False)
            node_sp(sp, n4, x3_tab, out, 4)
            for k in range(2):
                sp.wait_ge(n4.st[k], (NSTEPS // 2 + (k == 1)) * 16)

        @block.gpsimd
        def _(pool):
            for k in key_i:
                pool.memset(k[:, EC:COLS], NOKEY)
            pool.memset(wt[:, EC:COLS], 0.0).then_inc(s_init, 1)
            pool.memset(ident[:, :], 0.0).then_inc(s_ident, 1)
            pool.memset(before_f[:, :], 1.0).then_inc(s_before, 1)
            pool.memset(onecol[:, :], 0.0).then_inc(s_onecol, 1)
            pool.memset(fill_a, 0.0).then_inc(s_fillsrc, 1)
            pool.memset(fill_b, 0.0).then_inc(s_fillsrc, 1)
            pool.memset(ones[:, :], 1.0)
            pool.iota(iota[:, :], pattern=[[1, P]], base=0, channel_multiplier=0, allow_small_or_imprecise_dtypes=True)
            pool.iota(iota_p[:, :], pattern=[[0, 1]], base=0, channel_multiplier=1, allow_small_or_imprecise_dtypes=True)
            pool.iota(tile_no, pattern=[[1, TILES]], base=0, channel_multiplier=0, allow_small_or_imprecise_dtypes=True)
            pool.wait_ge(s_ident, 1)
            pool.affine_select(out=ident[:, :], in_=ident[:, :], compare_op=ALU.not_equal, fill=1.0, base=0,
                               pattern=[[-1, P]], channel_multiplier=1).then_inc(s_ident, 1)
            pool.wait_ge(s_before, 1)
            pool.affine_select(out=before_f[:, :], in_=before_f[:, :], compare_op=ALU.is_gt, fill=0.0, base=0,
                               pattern=[[1, P]], channel_multiplier=-1).then_inc(s_before, 1)
            pool.wait_ge(s_onecol, 1)
            pool.memset(onecol[:, P - 1:P], 1.0).then_inc(s_onecol, 1)
            pool.wait_ge(s_fillsrc, 2)
            pool.memset(fill_a[:, :, D:D + 1], -1.0).then_inc(s_fillsrc, 1)
            pool.memset(fill_b[:, :, 0:1], -1.0).then_inc(s_fillsrc, 1)

            def scatter(o, stage, table, with_attr):
                def step(s, k, u):
                    pool.wait_ge(s_fill, FILLED)
                    if with_attr:
                        pool.wait_ge((o.attr0, o.attr1)[k], u * 16 + 16)
                    pool.wait_ge(o.staged, s * 4 + (o.nth * STAGED + 4))
                    pool.sem_inc(pool_begun, 1)
                    for j in range(SG):
                        pool.indirect_dma_start(out=table, out_offset=bass.IndirectOffsetOnAxis(ap=stage_pos[:, k, j:j + 1], axis=0),
                                                in_=stage[:, k, j, :], in_offset=None).then_inc((o.scat0, o.scat1)[k], 16)
                run_steps(pool, SGROUPS, 2, 0, step)
                if with_attr:
                    pool.wait_ge(o.attr0, 16 * (SGROUPS // 2 + 1))
                pool.wait_ge(o.staged, (o.nth + 1) * STAGED)
                pool.indirect_dma_start(out=table, out_offset=bass.IndirectOffsetOnAxis(ap=stage_pos[0:ETAIL, 0, 0:1], axis=0),
                                        in_=stage[0:ETAIL, 0, 0, :], in_offset=None).then_inc(o.scatt, 16)
            STAGED = 4 * (SGROUPS + 1)
            FILLED = 16 * (TILES // FILL + 1)
            scatter(orders[0], stage_a, edges_a, True)
            scatter(orders[1], stage_b, edges_b, False)

            def gathers(p, table, width):
                def step(s, k, u):
                    pool.wait_ge(p.zero, p.nth + 1)
                    pool.wait_ge(p.idx, s * 2 + (2 * p.first + 1))
                    pool.sem_inc(pool_begun, 1)
                    for j in range(G):
                        at = (k * G + j) * width
                        pool.indirect_dma_start(out=rows[:, at:at + width], out_offset=None, in_=table,
                                                in_offset=bass.IndirectOffsetOnAxis(ap=idx[:, k, j:j + 1], axis=0)).then_inc(p.got[k], 16)
                run_steps(pool, GROUPS, RING, 0, step)

            def stored(n):
                for k in range(2):
                    pool.wait_ge(n.tab[k], NSTEPS // 2 * 16)
            pool.wait_ge(s_xpad, 32)
            gathers(p0, x_pad, D)
            stored(n0)
            gathers(p1, z_tab[0], H)
            pool.wait_ge(gin.tab, 16 * NSTEPS)
            gathers(p2, z_tab[1], H)
            stored(n2)
            gathers(p3, q_tab, D)
            stored(n3)
            gathers(p4, h_tab, HROW)

        @block.scalar
        def _(act):
            def stage(o, n, dest, fields):
                def step(s, k, u):
                    wait(act, (o.scat0, o.scat1)[k], u * (16 * SG))
                    for f, v in enumerate(fields):
                        act.activation(dest[:, k, :, dest.shape[3] - len(fields) + f], v[:, bass.ds(s * SG, SG)], ACT.Copy).then_inc(o.staged, 4 - len(fields) if f == 0 else 1)
                    act.activation(stage_pos[:, k, :], pos_i[n][:, bass.ds(s * SG, SG)], ACT.Copy).then_inc(o.staged, 1)
                act.wait_ge(o.ranked, n + 1)
                run_steps(act, SGROUPS, 2, 0, step)
                act.wait_ge(o.scat0, SGROUPS // 2 * 16 * SG)
                for f, v in enumerate(fields):
                    act.activation(dest[0:ETAIL, 0, 0:1, dest.shape[3] - len(fields) + f], v[0:ETAIL, EC:COLS], ACT.Copy).then_inc(o.staged, 4 - len(fields) if f == 0 else 1)
                act.activation(stage_pos[0:ETAIL, 0, 0:1], pos_i[n][0:ETAIL, EC:COLS], ACT.Copy).then_inc(o.staged, 1)
            act.wait_ge(s_keyin, 96)
            stage(orders[0], 0, stage_a, (lo_i[0], key_i[1], wt))
            act.wait_ge(orders[0].scat1, SGROUPS // 2 * 16 * SG)
            act.wait_ge(orders[0].scatt, 16)
            stage(orders[1], 1, stage_b, (lo_i[1], key_i[0]))

            def node_act(n, kind):
                sq = 2 if kind == 0 else 1

                def root(s, r):
                    w = BSTEP * (2 if kind == 0 and r == 0 else 1)
                    act.wait_ge(n.var, s * sq + r + 1)
                    act.activation(mom[6][:, 0:w], mom[5][:, 0:w], ACT.Sqrt).then_inc(n.std, 1)

                def evacuate(g, kk, gu):
                    act.wait_ge(n.ptr, g + 1)
                    act.activation(proj_t[:, kk], bank_slot(kk)[:, 0:BSTEP * D], ACT.Copy).then_inc(n.ptrc, 1)
                    if kind != 0:
                        wait(act, n.tab[kk], gu * 16)
                    act.wait_ge(n.pmm, g + 1)
                    if kind == 0:
                        act.activation(z_all[:, bass.ds(g * (BSTEP * H), BSTEP * H)], bank_slot(kk)[:, 0:BSTEP * H], ACT.Copy).then_inc(n.pev, 1)
                    else:
                        res = bank_slot(kk)[:, 0:BSTEP * 2 * D].rearrange("p (b f) -> p b f", f=2 * D)
                        if kind == 2:
                            act.activation(p_all[:, bass.ds(g * (BSTEP * D), BSTEP * D)].rearrange("p (b f) -> p b f", f=D), res[:, :, 0:D], ACT.Copy)
                            act.activation(tabrow[:, kk, 0:BSTEP * D].rearrange("p (b f) -> p b f", f=D), res[:, :, D:2 * D], ACT.Copy).then_inc(n.pev, 1)
                        else:
                            row = tabrow[:, kk].rearrange("p (b f) -> p b f", f=HROW)
                            act.activation(row[:, :, 0:D], res[:, :, 0:D], ACT.Copy)
                            act.activation(row[:, :, D + 1:D + 2], res[:, :, D:D + 1], ACT.Copy)
                            act.activation(a_all[:, bass.ds(g * BSTEP, BSTEP)], res[:, :, D + 1:D + 2].rearrange("p b o -> p (b o)"), ACT.Copy).then_inc(n.pev, 1)

                def step(s, k, u):
                    if kind != 2 and live(s, NSTEPS):
                        root(s, 0)
                    g, (kk, gu) = s - 1, back(k, u, 1, 2)
                    if kind != 4 and live(g, NSTEPS):
                        evacuate(g, kk, gu)
                    if kind == 2 and live(s, NSTEPS):
                        root(s, 0)

                def branches(s, k, u):
                    if live(s - 1, NSTEPS):
                        root(s - 1, 0)
                    if live(s - 2, NSTEPS):
                        evacuate(s - 2, k, u - 1)
                    if live(s, NSTEPS):
                        act.wait_ge(n.tr, s + 1)
                        wait(act, n.hmm, s - 1)
                        act.activation(feat_t[:, k].rearrange("p b f -> p (b f)"), bank_slot(k)[:, 0:BSTEP * 2 * D], ACT.Copy).then_inc(n.trc, 1)
                    if live(s - 1, NSTEPS):
                        root(s - 1, 1)
                    if live(s, NSTEPS):
                        act.wait_ge(n.hmm, s + 1)
                        wait(act, n.xnew, s - 1)
                        act.activation(hidn[:, k].rearrange("p b f -> p (b f)"), bank_slot(k)[:, 0:BSTEP * 2 * D], ACT.Relu).then_inc(n.relu, 1)
                if kind == 3:
                    act.wait_ge(n.one, 1)
                if kind == 0:
                    run_steps(act, NSTEPS, 2, 2, branches)
                else:
                    run_steps(act, NSTEPS, 2, 1, step)

            node_act(n0, 0)

            def gin_act(l):
                g = gin

                def relu(s, k, u):
                    act.wait_ge(g.tr, s + (l * NSTEPS + 1))
                    act.activation(h_all[:, bass.ds(s * (BSTEP * P), BSTEP * P)], bank_slot(k)[0:H, 0:BSTEP * P], ACT.Relu, bias=col_h[l][:, 0:1]).then_inc(g.relu, 1)
                run_steps(act, NSTEPS, 2, 0, relu)
                act.wait_ge(g.var, 2 * l + 1)
                act.activation(bn_cols[0:H, 3:4], bn_cols[0:H, 2:3], ACT.Sqrt).then_inc(g.std, 1)
                act.wait_ge(g.aff, 2 * l + 1)
                for c in range(5):
                    part = h_all[:, c * (N // 5):(c + 1) * (N // 5)]
                    act.activation(part, part, ACT.Identity, scale=bn_cols[0:H, 5:6], bias=bn_cols[0:H, 6:7]).then_inc(g.hbn, 1)

                def evac(s, k, u):
                    act.wait_ge(g.mm, s + (l * NCH + 1))
                    act.activation(y_all[:, bass.ds(s * CH, CH)], ps[:, k, 0:CH], ACT.Identity, bias=col_d[l][:, 0:1]).then_inc(g.ev, 1)
                run_steps(act, NCH, 5, 0, evac)
                act.wait_ge(g.var, 2 * l + 2)
                act.activation(bn_cols[:, 3:4], bn_cols[:, 2:3], ACT.Sqrt).then_inc(g.std, 1)
                act.wait_ge(g.aff, 2 * l + 2)
                for c in range(5):
                    part = y_all[:, c * (N // 5):(c + 1) * (N // 5)]
                    act.activation(part, part, ACT.Identity, scale=bn_cols[:, 5:6], bias=bn_cols[:, 6:7]).then_inc(g.ybn, 1)
                if l == 0:
                    def zout(s, k, u):
                        act.wait_ge(g.zmm, s + 1)
                        act.activation(z_all[:, bass.ds(s * (BSTEP * H), BSTEP * H)], bank_slot(k)[:, 0:BSTEP * H], ACT.Copy).then_inc(g.zev, 1)
                    run_steps(act, NSTEPS, 2, 0, zout)
            gin_act(0)
            gin_act(1)
            node_act(n2, 2)

            p = p3

            def mlp(s, k, u):
                if live(s, GROUPS):
                    act.wait_ge(p.tr, s + 1)
                    wait(act, p.hmm, s - 1)
                    act.activation(attr_t[:, k % 2], ps[:, k % 2, :], ACT.Copy).then_inc(p.trc, 1)
                g = s - 2
                if live(g, GROUPS):
                    act.wait_ge(p.hmm, g + 1)
                    wait(act, p.hid, g - 3)
                    kk = (k - 2) % 4
                    for j in range(G):
                        act.activation(square[:, j, :], hidden_bank(kk)[:, j * P:(j + 1) * P], ACT.Square, accum_out=spread[:, kk, 0, j:j + 1]).then_inc(p.var, 1)
                    act.wait_ge(p.var, g * G + G)
                    act.activation(spread[:, kk, 1, :], spread[:, kk, 0, :], ACT.Sqrt, scale=1.0 / D, bias=eps2[:, 0:1]).then_inc(p.std, 1)
                g, kk = s - 4, (k - 4) % 4
                if live(g, GROUPS):
                    act.wait_ge(p.hid, g + 1)
                    wait(act, p.mm, g - 1)
                    for j in range(G):
                        ins = act.activation(msg[:, kk % 2, j], hid[:, kk % 2, j], ACT.Relu, scale=spread[:, kk, 2, j:j + 1])
                    ins.then_inc(p.msg, 1)
            run_steps(act, GROUPS, RING, 4, mlp)
            node_act(n3, 3)

            p4_ = p4

            def expo(s, k, u):
                act.wait_ge(p4_.sc, s * 3 + 3)
                wait(act, p4_.oh, s - 1)
                act.activation(score[:, k % 2, 3, :], score[:, k % 2, 2, :], ACT.Exp).then_inc(p4_.exp, 1)
            run_steps(act, GROUPS, RING, 0, expo)
            node_act(n4, 4)

        @block.tensor
        def _(pe):
            pe.wait_ge(s_win, WIN)
            pe.wait_ge(s_ident, 2)
            for n in range(3):
                m = pe.transpose(ps[:, n, 0:P], raw[:, n, :], ident[:, :])
            m.then_inc(s_prep_mm, 1)
            pe.wait_ge(s_prep, 3)
            for c in range(2):
                m = pe.matmul(ps[:, 3, c:c + 1], lhsT=raw[:, 3, :], rhs=ka[:, 1 - c:2 - c], start=True, stop=True)
            m.then_inc(s_prep_mm, 1)
            pe.wait_ge(s_before, 3)
            pe.wait_ge(s_onecol, 2)
            pe.wait_ge(s_prep, PREP)

            def rank(o):
                def hist(s, k, u):
                    pe.wait_ge(o.eqh, s + (o.nth * NB + 1))
                    pe.sem_inc(pe_begun, 1)
                    for c, (at, w) in enumerate(CHUNKS):
                        m = pe.matmul(ps[:, c, 0:w], lhsT=onecol[:, bass.ds(P - 1 - s, P)], rhs=eq[:, k, at:at + w],
                                      start=isinstance(s, int) and s == 0, stop=True, skip_group_check=True)
                    m.then_inc(o.hist, 1)
                run_steps(pe, NB, 2, 0, hist)
                pe.wait_ge(o.nt, o.nth + 1)
                pe.matmul(ps[:, 7, 0:1], lhsT=before_f[:, :], rhs=small[:, 2:3], start=True, stop=True).then_inc(o.start, 1)
                pe.wait_ge(o.cmp, o.nth + 1)
                for c in range(4):
                    m = pe.matmul(ps[0:1, c, 0:TILES // 4], lhsT=onecol[0:NB, P - 1:P], rhs=cmp_tiles[0:NB, c * (TILES // 4):(c + 1) * (TILES // 4)], start=True, stop=True)
                m.then_inc(o.blkmm, 1)

                def place(s, k, u):
                    pe.wait_ge(o.eqp, s + (o.nth * NB + 1))
                    wait(pe, o.took, s + (o.nth * NB - 1))
                    for c, (at, w) in enumerate(CHUNKS):
                        pe.matmul(ps[:, 4 * k + c, 0:w], lhsT=before_h[:, :], rhs=eq[:, k, at:at + w], start=True, stop=False)
                        m = pe.matmul(ps[:, 4 * k + c, 0:w], lhsT=block_row[:, k, :], rhs=base[:, at:at + w], start=False, stop=True)
                    m.then_inc(o.pos, 1)
                run_steps(pe, NB, 2, 0, place)
            for o in orders:
                rank(o)
                pe.wait_ge(o.ranked, o.nth + 1)
            pe.wait_ge(s_pay_a, 64)
            w = TILES // 16
            for c in range(16):
                m = pe.transpose(ps[0:w, c // 4, (c % 4) * P:(c % 4 + 1) * P], pay_a[:, c * w:(c + 1) * w, 0], ident[:, :])
            m.then_inc(s_lot, 1)
            pe.wait_ge(s_lotc, 16)

            def sums(p, width):
                def step(s, k, u):
                    g, (kk, gu) = s - 1, back(k, u, 1, RING)
                    if live(g, GROUPS):
                        pe.wait_ge(p.oh, g + (p.first + 1))
                        pe.wait_ge(p.got[kk], gu * (16 * G) + (p.got0 + 16 * G))
                        wait(pe, p.acc, g * G + (p.first - 3) * G)
                        for j in range(G):
                            at = (kk * G + j) * width
                            m = pe.matmul(ps[:, kk % 4, j * width:(j + 1) * width], lhsT=onehot[:, kk % 4, j], rhs=rows[:, at:at + width], start=True, stop=True)
                        m.then_inc(p.mm, 1)
                run_steps(pe, GROUPS, RING, 1, step)

            def node_pe(n, kind):
                def step(s, k, u):
                    g, (kk, gu) = s - 1, back(k, u, 1, 2)
                    front = bank_slot(k)
                    if live(s, NSTEPS) and kind in (0, 2):
                        wait(pe, n.pev, s - 1)
                        if kind == 0:
                            pe.wait_ge(n.xl[k], u * 16 + 16)
                        for j in range(BSTEP):
                            if kind == 0:
                                pe.transpose(front[:, j * 2 * D:j * 2 * D + D], xin[:, k, j], ident[:, :])
                                m = pe.transpose(front[:, j * 2 * D + D:(j + 1) * 2 * D], acc[:, bass.ds(s * (BSTEP * D) + j * D, D)], ident[:, :])
                            else:
                                m = pe.transpose(front[:, j * D:(j + 1) * D], y_all[:, bass.ds(s * (BSTEP * P) + j * P, P)], ident[:, :])
                        m.then_inc(n.tr, 1)
                    if live(s, NSTEPS) and kind == 0:
                        pe.wait_ge(n.trc, s + 1)
                        for j in range(BSTEP):
                            for h, wgt in enumerate((ws_t, wn_t)):
                                at = slice(j * 2 * D + h * D, j * 2 * D + (h + 1) * D)
                                pe.matmul(front[:, at], lhsT=feat_t[:, k, j, h * D:(h + 1) * D], rhs=wgt[:, :], start=True, stop=False)
                                m = pe.matmul(front[:, at], lhsT=ones[0:1, :], rhs=bias0[:, h * D:(h + 1) * D], start=False, stop=True)
                        m.then_inc(n.hmm, 1)
                    if live(g, NSTEPS):
                        pe.wait_ge(n.xnew, g + 1)
                        if kind == 3:
                            wait(pe, n.pev, g - 1)
                        for j in range(BSTEP):
                            m = pe.transpose(bank_slot(kk)[:, j * D:(j + 1) * D], xnew[:, kk, j], ident[:, :])
                        m.then_inc(n.ptr, 1)
                    if live(g, NSTEPS):
                        pe.wait_ge(n.ptrc, g + 1)
                        res = bank_slot(kk)
                        for j in range(BSTEP):
                            feat = proj_t[:, kk, j * D:(j + 1) * D]
                            if kind == 0:
                                m = pe.matmul(res[:, j * H:(j + 1) * H], lhsT=feat, rhs=w1[0][:, :], start=True, stop=True)
                            elif kind == 2:
                                at = j * 2 * D
                                pe.matmul(res[:, at:at + D], lhsT=feat, rhs=wc[:, 0, :], start=True, stop=False)
                                pe.matmul(res[:, at:at + D], lhsT=ones[0:1, :], rhs=b2c[:, :], start=False, stop=True)
                                m = pe.matmul(res[:, at + D:at + 2 * D], lhsT=feat, rhs=wc[:, 1, :], start=True, stop=True)
                            else:
                                m = pe.matmul(res[:, j * 2 * D:j * 2 * D + HROW], lhsT=feat, rhs=kaug[:, :], start=True, stop=True)
                        m.then_inc(n.pmm, 1)
                if kind == 3:
                    run_steps(pe, NSTEPS, 2, 1, step)
                else:
                    write_out(NSTEPS, 2, 1, step)

            sums(p0, D)
            pe.wait_ge(p0.acc, TILES)
            node_pe(n0, 0)
            pe.wait_ge(n0.pev, NSTEPS)

            def gin_pe(l):
                g = gin
                pe.wait_ge(g.u, l + 1)

                def turn(s, k, u):
                    wait(pe, g.relu, s + (l * NSTEPS - 1))
                    for j in range(BSTEP):
                        m = pe.transpose(bank_slot(k)[0:H, j * P:(j + 1) * P], acc[:, bass.ds(s * (BSTEP * H) + j * H, H)], ident[:, :])
                    m.then_inc(g.tr, 1)
                write_out(NSTEPS, 2, 0, turn)

                def widen(s, k, u):
                    pe.wait_ge(g.hbn, (5 * l + 1) + (s // 5 if isinstance(s, int) else u))
                    wait(pe, g.ev, s + (l * NCH - 4))
                    pe.matmul(ps[:, k, 0:CH], lhsT=w2[l][:, :], rhs=h_all[:, bass.ds(s * CH, CH)], start=True, stop=True).then_inc(g.mm, 1)
                run_steps(pe, NCH, 5, 0, widen)
                if l == 1:
                    pe.wait_ge(g.act, 10)
                else:
                    def narrow(s, k, u):
                        pe.wait_ge(g.act, min(5, -(-(s + 1) * BSTEP * P // (N // 5))))
                        wait(pe, g.zev, s - 1)
                        for j in range(BSTEP):
                            m = pe.matmul(bank_slot(k)[:, j * H:(j + 1) * H], lhsT=y_all[:, bass.ds(s * (BSTEP * P) + j * P, P)], rhs=w1[1][:, :], start=True, stop=True)
                        m.then_inc(g.zmm, 1)
                    write_out(NSTEPS, 2, 0, narrow)
                    pe.wait_ge(g.zev, NSTEPS)
            sums(p1, H)
            gin_pe(0)
            sums(p2, H)
            gin_pe(1)
            node_pe(n2, 2)
            pe.wait_ge(n2.pev, NSTEPS)

            p = p3

            def mlp(s, k, u):
                if live(s, GROUPS):
                    pe.wait_ge(p.attr[k % 4], u * 32 + (k // 4 * 16 + 16))
                    wait(pe, p.trc, s - 1)
                    for j in range(G):
                        m = pe.transpose(ps[:, k % 2, j * P:(j + 1) * P], attr[:, k % 4, j], ident[:, :])
                    m.then_inc(p.tr, 1)
                g, (kk, gu) = s - 1, back(k, u, 1, RING)
                if live(g, GROUPS):
                    bl = load_blocks(ONLY_PE, blk_a, g)
                    pe.wait_ge(p.trc, g + 1)
                    pe.wait_ge(p.oht, g + 1)
                    pe.wait_ge(p.got[kk], gu * (16 * G) + (p.got0 + 16 * G))
                    wait(pe, p.std, g - 3)
                    wait(pe, p.hid, g - 3)
                    for j in range(G):
                        o = hidden_bank(kk)[:, j * P:(j + 1) * P]
                        at = (kk * G + j) * D
                        pe.matmul(o, lhsT=attr_t[:, kk % 2, j * P:(j + 1) * P], rhs=wc[:, 2, :], start=True, stop=False)
                        pe.matmul(o, lhsT=ident[:, :], rhs=rows[:, at:at + D], start=False, stop=False)
                        m = pe.matmul(o, lhsT=onehot_t[:, kk % 2, j * P:(j + 1) * P], rhs=p_all[:, bass.ds(bl[j] * D, D)], start=False, stop=True)
                    m.then_inc(p.hmm, 1)
                g, kk = s - 5, (k - 5) % RING
                if live(g, GROUPS):
                    pe.wait_ge(p.oh, g + 1)
                    pe.wait_ge(p.msg, g + 1)
                    wait(pe, p.acc, g * G - G)
                    for j in range(G):
                        m = pe.matmul(ps[:, 4 + kk % 2, j * P:(j + 1) * P], lhsT=onehot[:, kk % 4, j], rhs=msg[:, kk % 2, j], start=True, stop=True)
                    m.then_inc(p.mm, 1)
            run_steps(pe, GROUPS, RING, 5, mlp)
            pe.wait_ge(p3.acc, TILES)
            node_pe(n3, 3)
            pe.wait_ge(n3.pev, NSTEPS)

            q = p4

            def attend(s, k, u):
                g, (kk, gu) = s - 1, back(k, u, 1, RING)
                if live(g, GROUPS):
                    bl = load_blocks(ONLY_PE, blk_a, g)
                    pe.wait_ge(q.oht, g + 1)
                    wait(pe, q.sc, g * 3 - 5)
                    for j in range(G):
                        m = pe.matmul(ps[:, kk % 2, j:j + 1], lhsT=onehot_t[:, kk % 2, j * P:(j + 1) * P], rhs=a_all[:, bass.ds(bl[j], 1)], start=True, stop=True)
                    m.then_inc(q.smm, 1)
                g, (kk, gu) = s - 4, back(k, u, 4, RING)
                if live(g, GROUPS):
                    pe.wait_ge(q.oh, g + 1)
                    pe.wait_ge(q.got[kk], gu * (16 * G) + (q.got0 + 16 * G))
                    wait(pe, q.acc, g * G - G)
                    for j in range(G):
                        at = (kk * G + j) * HROW
                        m = pe.matmul(ps[:, 2 + 2 * (kk % 2) + j // 2, (j % 2) * 256:(j % 2) * 256 + D + 1], lhsT=onehot[:, kk % 4, j], rhs=rows[:, at:at + D + 1], start=True, stop=True)
                    m.then_inc(q.mm, 1)
            run_steps(pe, GROUPS, RING, 4, attend)

        @block.vector
        def _(dve):
            ch = Chain(dve, s_prep)
            ch.begin(0)
            dve.wait_ge(s_prep_mm, 1)
            for n, v in enumerate((ws_t, wn_t)):
                ch.post(dve.tensor_copy(v[:, :], ps[:, n, 0:P]))
            ch.post(dve.tensor_copy(raw[:, 3, :], ps[:, 2, 0:P]))
            dve.wait_ge(s_win, WIN)
            dve.tensor_tensor(offs0[:, :], raw_offs[:, 0:D], raw_offs[:, D:2 * D], ALU.add)
            dve.memset(eps2[:, :], 1e-5)
            dve.wait_ge(s_before, 2)
            dve.tensor_copy(before_h[:, :], before_f[:, :]).then_inc(s_before, 1)
            ch.post(dve.tensor_reduce(small[:, 0:3], wc[:, :, :], mybir.AxisListType.X, ALU.add))
            ch(dve.tensor_reduce(small[0:1, 3:4], b2c[:, :], mybir.AxisListType.X, ALU.add))
            ch(dve.tensor_scalar(small[:, 4:7], small[:, 0:3], 1.0 / D, None, ALU.mult))
            ch(dve.tensor_scalar(small[0:1, 7:8], small[0:1, 3:4], 1.0 / D, None, ALU.mult))
            for n in range(3):
                dve.tensor_scalar(wc[:, n, :], wc[:, n, :], small[:, 4 + n:5 + n], None, ALU.subtract)
            ch(dve.tensor_scalar(b2c[:, :], b2c[:, :], small[0:1, 7:8], None, ALU.subtract))
            dve.wait_ge(s_prep_mm, 2)
            ch(dve.tensor_copy(kaug[:, D:D + 2], ps[:, 3, 0:2]))
            ch(dve.memset(pos_f, 0.0))
            ch(dve.memset(small[:, :], 0.0))
            assert ch.n == PREP, ch.n
            dve.wait_ge(s_keyin, 96)
            ch = Chain(dve, s_sort)

            def rank(n, o):
                ch.post(dve.tensor_scalar(hi_i, key_i[n], 7, None, ALU.arith_shift_right))
                ch(dve.tensor_scalar(lo_i[n], key_i[n], P - 1, None, ALU.bitwise_and))
                assert NB <= 256
                ch(dve.tensor_copy(hi_h, hi_i))

                def hist(s, k, u):
                    wait(dve, o.hist, s + (n * NB - 1))
                    dve.tensor_scalar(eq[:, k, 0:COLS], hi_h, iota[:, bass.ds(s, 1)], None, ALU.is_equal).then_inc(o.eqh, 1)
                run_steps(dve, NB, 2, 0, hist)
                dve.wait_ge(o.hist, (n + 1) * NB)
                counts = bank_slot(0)[:, 0:COLS]
                ch.post(dve.tensor_copy(base, counts))
                ch(dve.tensor_copy(scan[0], counts))
                cur, step = 0, 1
                while step < COLS:
                    a, z = scan[cur], scan[1 - cur]
                    ch.post(dve.tensor_tensor(z[:, step:], a[:, step:], a[:, :COLS - step], ALU.add))
                    ch(dve.tensor_copy(z[:, :step], a[:, :step]))
                    cur, step = 1 - cur, 2 * step
                total = scan[cur]
                ch(dve.tensor_scalar(small_i[:, 0:1], total[:, COLS - 1:COLS], float(P - 1), None, ALU.add))
                ch(dve.tensor_scalar(small_i[:, 1:2], small_i[:, 0:1], 7, None, ALU.arith_shift_right))
                dve.tensor_copy(small[:, 2:3], small_i[:, 1:2]).then_inc(o.nt, 1)
                ch(dve.tensor_tensor(base, total, base, ALU.subtract))
                dve.wait_ge(o.start, n + 1)
                ch.post(dve.tensor_copy(small[:, 3:4], ps[:, 7, 0:1]))
                ch(dve.tensor_scalar(small[:, 4:5], ps[:, 7, 0:1], float(P), None, ALU.mult))
                dve.tensor_scalar(cmp_tiles[0:NB, :], tile_no[0:NB, :], small[0:NB, 3:4], None, ALU.is_ge).then_inc(o.cmp, 1)
                ch(dve.tensor_scalar(base, base, small[:, 4:5], None, ALU.add))
                dve.wait_ge(o.blkmm, n + 1)
                dest = blk_a[0:1, :] if n == 0 else tile_no.bitcast(I32)[0:1, :]
                ch(dve.tensor_scalar(dest.rearrange("p (c t) -> p c t", c=4), ps[0:1, 0:4, 0:TILES // 4], -1.0, None, ALU.add))

                def place(s, k, u):
                    if live(s, NB):
                        wait(dve, o.took, s + (n * NB - 1))
                        dve.tensor_copy(block_row[:, k, :], ident[:, bass.ds(s, 1)].to_broadcast([P, P]))
                        dve.tensor_scalar(eq[:, k, 0:COLS], hi_h, iota[:, bass.ds(s, 1)], None, ALU.is_equal).then_inc(o.eqp, 1)
                    g, kk = s - 1, 1 - k
                    if live(g, NB):
                        dve.wait_ge(o.pos, g + (n * NB + 1))
                        wait(dve, o.took, g + n * NB)
                        dve.sem_inc(dve_begun, 1)
                        dve.copy_predicated(pos_f, eq[:, kk, 0:COLS].bitcast(U16), bank_slot(kk)[:, 0:COLS]).then_inc(o.took, 1)
                run_steps(dve, NB, 2, 1, place)
                dve.wait_ge(o.took, (n + 1) * NB)
                ch(dve.tensor_copy(pos_i[n], pos_f))
                ch(dve.tensor_scalar(hi_i, pos_i[n], 7, None, ALU.arith_shift_right))
                ch(dve.tensor_scalar(pos_i[n], pos_i[n], P - 1, None, ALU.bitwise_and))
                ch(dve.scalar_tensor_tensor(out=pos_i[n], in0=pos_i[n], scalar=float(TILES), in1=hi_i, op0=ALU.mult, op1=ALU.add))
                dve.memset(small[:, 8:9], 0.0).then_inc(o.ranked, 1)
            for n, o in enumerate(orders):
                rank(n, o)
            dve.wait_ge(s_lot, 1)
            for c in range(16):
                dve.tensor_copy(lot_tmp[:, c, :], ps[0:TILES // 16, c // 4, (c % 4) * P:(c % 4 + 1) * P]).then_inc(s_lotc, 1)
            dve.wait_ge(s_lost, 16)
            dve.wait_ge(s_blkst, 16)
            o = orders[1]
            dve.wait_ge(o.scat0, SGROUPS // 2 * 16 * SG)
            dve.wait_ge(o.scat1, SGROUPS // 2 * 16 * SG)
            dve.wait_ge(o.scatt, 32)

            AHEAD = 2

            def stage_edges(p, pay, s, k):
                nf = pay.shape[2]
                dve.tensor_copy(idx[:, k, :], pay[:, bass.ds(s * G, G), 1]).then_inc(p.idx, 1)
                dve.tensor_copy(pst[:, k, :, 0:nf], pay[:, bass.ds(s * G, G), :]).then_inc(p.idx, 1)

            def weighted_onehot(p, k, j, scale):
                ins = dve.tensor_scalar(onehot[:, k % 4, j], iota[:, :], pst[:, k, j, 0:1], scale, ALU.is_equal, ALU.mult)
                if j == G - 1:
                    ins.then_inc(p.oh, 1)

            def add_tile(p, bl, g, j, pitch, width, tile_sums):
                wait(dve, p.acc, g * G + (p.first * G + j))
                o = acc[:, bass.ds(bl[j] * pitch, width)]
                dve.tensor_tensor(o, o, tile_sums, ALU.add).then_inc(p.acc, 1)

            def plain_onehot(p, k):
                dve.tensor_tensor(onehot[:, k % 4], iota[:, :].unsqueeze(1).to_broadcast([P, G, P]),
                                  pst[:, k, :, 0:1].to_broadcast([P, G, P]), ALU.is_equal).then_inc(p.oh, 1)

            def zero_acc(p, words):
                dve.memset(acc[:, 0:words], 0.0).then_inc(p.zero, 1)
                dve.wait_ge(p.zero, p.nth + 1)

            def sums(p, pay, blk, width, weighted):
                def step(s, k, u):
                    if live(s, GROUPS):
                        stage_edges(p, pay, s, k)
                        dve.wait_ge(p.idx, s * 2 + (2 * p.first + 2))
                        if weighted:
                            for j in range(G):
                                weighted_onehot(p, k, j, pst[:, k, j, 2:3])
                        else:
                            plain_onehot(p, k)
                    g, kk = s - 2, (k - 2) % 4
                    if live(g, GROUPS):
                        bl = load_blocks(ONLY_DVE, blk, g)
                        dve.wait_ge(p.mm, g + (p.first + 1))
                        for j in range(G):
                            add_tile(p, bl, g, j, width, width, ps[:, kk, j * width:(j + 1) * width])
                run_steps(dve, GROUPS, RING, 2, step)
                dve.wait_ge(p.acc, p.first * G + TILES)

            dve.wait_ge(s_pay_a, 64)
            zero_acc(p0, NP)
            sums(p0, pay_a, blk_a, D, True)

            def mean_var(c, w, eps):
                st = [stats[:, 0:w, f] for f in range(6)]
                m = [v[:, 0:w] for v in mom]
                c.post(dve.tensor_tensor(m[0], st[1], st[4], ALU.add))
                c.post(dve.tensor_tensor(m[1], st[1], st[4], ALU.subtract))
                c(dve.tensor_tensor(m[2], st[2], st[5], ALU.add))
                c.post(dve.tensor_scalar(m[4], m[0], 0.5, None, ALU.mult))
                c.post(dve.scalar_tensor_tensor(out=m[3], in0=m[1], scalar=0.25, in1=m[1], op0=ALU.mult, op1=ALU.mult))
                c(dve.tensor_scalar(m[2], m[2], 1.0 / D, eps, ALU.mult, ALU.add))
                c.post(dve.tensor_tensor(m[5], m[2], m[3], ALU.add))

            def node_dve(n, kind):
                c = Chain(dve, n.ch)
                count = {0: 18 + 24, 2: 13, 3: 13, 4: 16}[kind]
                roots = 2 if kind == 0 else 1

                def deviation(s, r, w):
                    dve.wait_ge(n.std, s * roots + r + 1)
                    c(dve.reciprocal(mom[7][:, 0:w], mom[6][:, 0:w]))

                def step(s, k, u):
                    c.begin(s * COUNT)
                    h, xn = hidn[:, k], xnew[:, k]
                    if kind == 0:
                        w = 2 * BSTEP
                        dve.wait_ge(n.relu, s + 1)
                        for j in range(w):
                            ins = dve.bn_stats(stats[:, j, :], h[:, j // 2, (j % 2) * D:(j % 2 + 1) * D])
                        c(ins)
                        mean_var(c, w, 1e-9)
                        dve.memset(small[:, 10:11], 0.0).then_inc(n.var, 1)
                        deviation(s, 0, w)
                        for j in range(w):
                            v = h[:, j // 2, (j % 2) * D:(j % 2 + 1) * D]
                            ins = dve.tensor_scalar(v, v, mom[4][:, j:j + 1], mom[7][:, j:j + 1], ALU.subtract, ALU.mult)
                        c(ins)
                        c(dve.tensor_tensor(h, h, scale0[:, :].unsqueeze(1).to_broadcast([P, BSTEP, 2 * D]), ALU.mult))
                    wait(dve, n.st[k], u * 16)
                    if kind != 4:
                        wait(dve, n.ptr, s - 1)
                    if kind == 0:
                        c(dve.tensor_tensor(xn, h[:, :, 0:D], h[:, :, D:2 * D], ALU.add))
                        dve.wait_ge(n.xl[k], u * 16 + 16)
                        c(dve.tensor_tensor(xn, xn, xin[:, k], ALU.add))
                        c(dve.tensor_tensor(xn, xn, offs0[:, :].unsqueeze(1).to_broadcast([P, BSTEP, D]), ALU.add))
                    elif kind == 2:
                        dve.wait_ge(n.tr, s + 1)
                        dve.wait_ge(n.xl[k], u * 16 + 16)
                        c(dve.tensor_tensor(xn, bank_slot(k)[:, 0:BSTEP * D].rearrange("p (b f) -> p b f", f=D), xin[:, k], ALU.add))
                    elif kind == 3:
                        dve.wait_ge(n.xl[k], u * 16 + 16)
                        c(dve.tensor_tensor(xn, acc[:, bass.ds(s * (BSTEP * D), BSTEP * D)].rearrange("p (b f) -> p b f", f=D), xin[:, k], ALU.add))
                    else:
                        at = acc[:, bass.ds(s * (BSTEP * ACCW), BSTEP * ACCW)].rearrange("p (b f) -> p b f", f=ACCW)
                        c(dve.tensor_scalar(mom[0][:, 0:BSTEP], at[:, :, D], 1e-7, None, ALU.add))
                        c(dve.reciprocal(mom[1][:, 0:BSTEP], mom[0][:, 0:BSTEP]))
                        c(dve.tensor_tensor(xn, at[:, :, 0:D], mom[1][:, 0:BSTEP].unsqueeze(2).to_broadcast([P, BSTEP, D]), ALU.mult))
                        dve.wait_ge(n.xl[k], u * 16 + 16)
                        c(dve.tensor_tensor(xn, xn, xin[:, k], ALU.add))
                    for j in range(BSTEP):
                        ins = dve.bn_stats(stats[:, j, :], xn[:, j])
                    c(ins)
                    mean_var(c, BSTEP, 1e-5)
                    dve.memset(small[:, 11:12], 0.0).then_inc(n.var, 1)
                    deviation(s, roots - 1, BSTEP)
                    for j in range(BSTEP):
                        ins = dve.tensor_scalar(xn[:, j], xn[:, j], mom[4][:, j:j + 1], mom[7][:, j:j + 1], ALU.subtract, ALU.mult)
                    ins.then_inc(n.xnew, 1)
                    assert c.n == COUNT, (kind, c.n, COUNT)
                COUNT = {0: 23, 2: 10, 3: 10, 4: 13}[kind]
                if kind == 3:
                    dve.memset(tabrow, 1.0).then_inc(n.one, 1)
                run_steps(dve, NSTEPS, 2, 0, step)
                dve.wait_ge(n.xnew, NSTEPS)

            node_dve(n0, 0)

            GIN_CHAIN = 10

            def gin_dve(l):
                g = gin
                c = Chain(dve, g.ch)
                c.begin(l * GIN_CHAIN)
                dve.tensor_tensor(acc[:, 0:NB * H], acc[:, 0:NB * H], z_all, ALU.add).then_inc(g.u, 1)

                def affine(part, done, cols, gain, shift):
                    c(dve.bn_aggr(cols[:, 0:2], part))
                    dve.tensor_scalar(cols[:, 2:3], cols[:, 1:2], 1e-5, None, ALU.add).then_inc(g.var, 1)
                    dve.wait_ge(g.std, 2 * l + done)
                    c(dve.reciprocal(cols[:, 4:5], cols[:, 3:4]))
                    c(dve.tensor_tensor(cols[:, 5:6], cols[:, 4:5], gain, ALU.mult))
                    c(dve.tensor_tensor(cols[:, 7:8], cols[:, 0:1], cols[:, 5:6], ALU.mult))
                    dve.tensor_tensor(cols[:, 6:7], shift, cols[:, 7:8], ALU.subtract).then_inc(g.aff, 1)

                for n in range(NCH):
                    dve.wait_ge(g.relu, l * NSTEPS + min(NSTEPS, -(-(n + 1) * CH // (BSTEP * P))))
                    ins = dve.bn_stats(bn_part[0:H, n, :], h_all[:, n * CH:(n + 1) * CH])
                c(ins)
                affine(bn_part[0:H].rearrange("p n f -> p (n f)"), 1, bn_cols[0:H], col_h[l][:, 1:2], col_h[l][:, 2:3])
                dve.memset(y_all[:, N:NP], 0.0)
                dve.wait_ge(g.hbn, 5 * l + 5)
                for n in range(NCH):
                    dve.wait_ge(g.ev, l * NCH + n + 1)
                    ins = dve.bn_stats(bn_part[:, n, :], y_all[:, n * CH:(n + 1) * CH])
                c(ins)
                affine(bn_part.rearrange("p n f -> p (n f)"), 2, bn_cols, col_d[l][:, 1:2], col_d[l][:, 2:3])
                assert c.n == GIN_CHAIN, c.n
                for n in range(5):
                    part = y_all[:, n * (N // 5):(n + 1) * (N // 5)]
                    dve.wait_ge(g.ybn, 5 * l + n + 1)
                    dve.scalar_tensor_tensor(out=part, in0=part, scalar=0.01, in1=part, op0=ALU.mult, op1=ALU.max).then_inc(g.act, 1)

            dve.wait_ge(s_pay_b, 32)
            dve.wait_ge(n0.pev, NSTEPS)
            dve.wait_ge(n0.hmm, NSTEPS)
            zero_acc(p1, NB * H)
            sums(p1, pay_b, blk_b, H, False)
            gin_dve(0)
            dve.wait_ge(gin.zev, NSTEPS)
            zero_acc(p2, NB * H)
            sums(p2, pay_b, blk_b, H, False)
            gin_dve(1)
            node_dve(n2, 2)

            p = p3
            dve.wait_ge(n2.pev, NSTEPS)
            for k in range(2):
                dve.wait_ge(n2.st[k], NSTEPS // 2 * 16)
                dve.wait_ge(n2.tab[k], NSTEPS // 2 * 16)
            zero_acc(p, NP)

            def turned_onehot(p, k, u):
                dve.wait_ge(p.lo[k % 4], u * 32 + (p.lo0 + k // 4 * 16 + 16))
                dve.tensor_scalar(onehot_t[:, k % 2], lo_bc[:, k % 4], iota_p[:, 0:1], None, ALU.is_equal).then_inc(p.oht, 1)

            def mlp(s, k, u):
                turn, (kt, ut) = s - AHEAD, back(k, u, AHEAD, RING)
                g, kk = s - (AHEAD + 3), (k - (AHEAD + 3)) % RING
                done, kd = s - (AHEAD + 6), (k - (AHEAD + 6)) % 2
                if live(done, GROUPS):
                    bl = load_blocks(ONLY_DVE, blk_a, done)

                def add(j):
                    if live(done, GROUPS):
                        add_tile(p, bl, done, j, D, D, ps[:, 4 + kd, j * P:(j + 1) * P])
                std = spread[:, kk % 4, 1, :]

                def shift(j):
                    v = hid[:, kk % 2, j]
                    return dve.scalar_tensor_tensor(out=v, in0=beta2[:, :], scalar=std[:, j:j + 1], in1=v, op0=ALU.mult, op1=ALU.add)

                if live(s, GROUPS):
                    stage_edges(p, pay_a, s, k)
                if live(turn, GROUPS):
                    wait(dve, p.hmm, turn - 1)
                    turned_onehot(p, kt, ut)
                if live(done, GROUPS):
                    dve.wait_ge(p.mm, done + 1)
                add(0)
                if live(g, GROUPS):
                    dve.wait_ge(p.std, g + 1)
                    wait(dve, p.msg, g - 1)
                    dve.reciprocal(spread[:, kk % 4, 2, :], std).then_inc(p.hch, 1)
                    dve.tensor_tensor(hid[:, kk % 2], hidden_bank(kk).rearrange("p (j f) -> p j f", f=D),
                                      gamma2[:, :].unsqueeze(1).to_broadcast([P, G, D]), ALU.mult).then_inc(p.hch, 1)
                add(1)
                if live(g, GROUPS):
                    plain_onehot(p, kk)
                add(2)
                if live(g, GROUPS):
                    dve.wait_ge(p.hch, g * 2 + 2)
                    shift(0)
                    shift(1)
                add(3)
                if live(g, GROUPS):
                    shift(2)
                    shift(3).then_inc(p.hid, 1)
            run_steps(dve, GROUPS, RING, AHEAD + 6, mlp)
            dve.wait_ge(p.acc, TILES)
            node_dve(n3, 3)

            q = p4
            dve.wait_ge(n3.pev, NSTEPS)
            for k in range(2):
                dve.wait_ge(n3.st[k], NSTEPS // 2 * 16)
                dve.wait_ge(n3.tab[k], NSTEPS // 2 * 16)
            zero_acc(q, NB * ACCW)

            def attend(s, k, u):
                turn, (kt, ut) = s - AHEAD, back(k, u, AHEAD, RING)
                g, (kk, gu) = s - (AHEAD + 2), back(k, u, AHEAD + 2, RING)
                done, kd = s - (AHEAD + 5), (k - (AHEAD + 5)) % 2
                if live(done, GROUPS):
                    bl = load_blocks(ONLY_DVE, blk_a, done)
                if live(s, GROUPS):
                    stage_edges(q, pay_a, s, k)
                if live(turn, GROUPS):
                    wait(dve, q.smm, turn - 1)
                    turned_onehot(q, kt, ut)
                if live(g, GROUPS):
                    sc = [score[:, kk % 2, f, :] for f in range(4)]
                    other = rows[:, kk * G * HROW:(kk + 1) * G * HROW].rearrange("p (j f) -> p j f", f=HROW)[:, :, D + 1]
                    dve.wait_ge(q.smm, g + 1)
                    dve.wait_ge(q.got[kk], gu * (16 * G) + (q.got0 + 16 * G))
                    dve.tensor_tensor(sc[0], ps[:, kk % 2, 0:G], other, ALU.add).then_inc(q.sc, 1)
                    dve.wait_ge(q.sc, g * 3 + 1)
                    dve.scalar_tensor_tensor(out=sc[1], in0=sc[0], scalar=0.2, in1=sc[0], op0=ALU.mult, op1=ALU.max).then_inc(q.sc, 1)
                    dve.wait_ge(q.sc, g * 3 + 2)
                    wait(dve, q.exp, g - 1)
                    dve.tensor_scalar(sc[2], sc[1], -2.0, 2.0, ALU.max, ALU.min).then_inc(q.sc, 1)
                g, (kk3, _) = s - (AHEAD + 3), back(k, u, AHEAD + 3, RING)
                if live(g, GROUPS):
                    dve.wait_ge(q.exp, g + 1)
                if live(done, GROUPS):
                    dve.wait_ge(q.mm, done + 1)
                for j in range(G):
                    if live(done, GROUPS):
                        add_tile(q, bl, done, j, ACCW, D + 1, ps[:, 2 + 2 * kd + j // 2, (j % 2) * 256:(j % 2) * 256 + D + 1])
                    if live(g, GROUPS):
                        weighted_onehot(q, kk3, j, score[:, kk3 % 2, 3, j:j + 1])
            run_steps(dve, GROUPS, RING, AHEAD + 5, attend)
            dve.wait_ge(q.acc, TILES)
            node_dve(n4, 4)


_INS = ["x", "src", "dst", "edge_attr_128", "edge_weight",
        "L0_gnn_W_self", "L0_gnn_b_self", "L0_gnn_W_neigh", "L0_gnn_b_neigh", "L0_gnn_scale", "L0_gnn_offset",
        "L1_gnn_W1_0", "L1_gnn_b1_0", "L1_gnn_g1_0", "L1_gnn_be1_0", "L1_gnn_W2_0", "L1_gnn_b2_0", "L1_gnn_g2_0", "L1_gnn_be2_0",
        "L1_gnn_W1_1", "L1_gnn_b1_1", "L1_gnn_g1_1", "L1_gnn_be1_1", "L1_gnn_W2_1", "L1_gnn_b2_1", "L1_gnn_g2_1", "L1_gnn_be2_1",
        "L2_gnn_W", "L2_gnn_b", "L2_gnn_gamma", "L2_gnn_beta", "L3_gnn_kernel", "L3_gnn_kernel_attention"]


def kernel(**inputs):
    import numpy as _np
    import concourse.bacc as _bacc
    from concourse import mybir as _mybir
    from concourse.bass_utils import run_bass_kernel_spmd as _run

    nc = _bacc.Bacc("TRN2", target_bir_lowering=False, num_devices=1)
    arrays, args = {}, {}
    for name in _INS:
        a = _np.ascontiguousarray(inputs[name])
        arrays[f"in_{name}_dram"] = a
        args[name] = nc.dram_tensor(f"in_{name}_dram", a.shape, _mybir.dt.from_np(a.dtype), kind="ExternalInput").ap()
    out = nc.dram_tensor("out_0_dram", inputs["x"].shape, _mybir.dt.float32, kind="ExternalOutput").ap()
    gnn_program(nc, args, out)
    r = _run(nc, [arrays], core_ids=[0])
    return r.results[0]["out_0_dram"]
```
